# Optimizing a Trainium2 kernel written in Bass

```python
import numpy as np
import jax
import jax.numpy as jnp

def _softmax(x, axis=-1):
    return jax.nn.softmax(x, axis=axis)

def _gelu(x):
    return jax.nn.gelu(x, approximate=True)

def _silu(x):
    return jax.nn.silu(x)

def _sigmoid(x):
    return jax.nn.sigmoid(x)

def _layernorm(x, axis=-1, eps=1e-05):
    m = jnp.mean(x, axis=axis, keepdims=True)
    v = jnp.var(x, axis=axis, keepdims=True)
    return (x - m) / jnp.sqrt(v + eps)

def _scatter_add(tgt, idx, src, axis=0):
    return tgt.at[idx].add(src)

def _segment_sum(src, seg, n):
    return jax.ops.segment_sum(src, seg, n)
kernel_name = 'mk_dlrm_tower_d1_rec_r8_502266'

def setup_inputs(seed: int=0):
    np.random.seed(seed)
    _w = jnp.asarray

    def _rec_inputs():
        import jax
        import jax.numpy as jnp
        _tk = jax.random.key(seed)
        ids = jnp.stack([jax.random.randint(jax.random.fold_in(_tk, 200 + f), (512,), 0, v, jnp.int32) for f, v in enumerate([1000, 12500, 1250, 1000, 1000, 1000, 125000, 1000, 1250, 12500, 1250, 1000, 12500, 12500, 12500, 1000, 12500, 1000, 1000, 1000, 12500, 1000, 1250, 1250, 1250, 1250])], axis=1)
        tbl_0 = 0.05 * jax.random.normal(jax.random.fold_in(_tk, 500 + 0), (1000, 128), jnp.float32)
        tbl_1 = 0.05 * jax.random.normal(jax.random.fold_in(_tk, 500 + 1), (12500, 128), jnp.float32)
        tbl_2 = 0.05 * jax.random.normal(jax.random.fold_in(_tk, 500 + 2), (1250, 128), jnp.float32)
        tbl_3 = 0.05 * jax.random.normal(jax.random.fold_in(_tk, 500 + 3), (1000, 128), jnp.float32)
        tbl_4 = 0.05 * jax.random.normal(jax.random.fold_in(_tk, 500 + 4), (1000, 128), jnp.float32)
        tbl_5 = 0.05 * jax.random.normal(jax.random.fold_in(_tk, 500 + 5), (1000, 128), jnp.float32)
        tbl_6 = 0.05 * jax.random.normal(jax.random.fold_in(_tk, 500 + 6), (125000, 128), jnp.float32)
        tbl_7 = 0.05 * jax.random.normal(jax.random.fold_in(_tk, 500 + 7), (1000, 128), jnp.float32)
        tbl_8 = 0.05 * jax.random.normal(jax.random.fold_in(_tk, 500 + 8), (1250, 128), jnp.float32)
        tbl_9 = 0.05 * jax.random.normal(jax.random.fold_in(_tk, 500 + 9), (12500, 128), jnp.float32)
        tbl_10 = 0.05 * jax.random.normal(jax.random.fold_in(_tk, 500 + 10), (1250, 128), jnp.float32)
        tbl_11 = 0.05 * jax.random.normal(jax.random.fold_in(_tk, 500 + 11), (1000, 128), jnp.float32)
        tbl_12 = 0.05 * jax.random.normal(jax.random.fold_in(_tk, 500 + 12), (12500, 128), jnp.float32)
        tbl_13 = 0.05 * jax.random.normal(jax.random.fold_in(_tk, 500 + 13), (12500, 128), jnp.float32)
        tbl_14 = 0.05 * jax.random.normal(jax.random.fold_in(_tk, 500 + 14), (12500, 128), jnp.float32)
        tbl_15 = 0.05 * jax.random.normal(jax.random.fold_in(_tk, 500 + 15), (1000, 128), jnp.float32)
        tbl_16 = 0.05 * jax.random.normal(jax.random.fold_in(_tk, 500 + 16), (12500, 128), jnp.float32)
        tbl_17 = 0.05 * jax.random.normal(jax.random.fold_in(_tk, 500 + 17), (1000, 128), jnp.float32)
        tbl_18 = 0.05 * jax.random.normal(jax.random.fold_in(_tk, 500 + 18), (1000, 128), jnp.float32)
        tbl_19 = 0.05 * jax.random.normal(jax.random.fold_in(_tk, 500 + 19), (1000, 128), jnp.float32)
        tbl_20 = 0.05 * jax.random.normal(jax.random.fold_in(_tk, 500 + 20), (12500, 128), jnp.float32)
        tbl_21 = 0.05 * jax.random.normal(jax.random.fold_in(_tk, 500 + 21), (1000, 128), jnp.float32)
        tbl_22 = 0.05 * jax.random.normal(jax.random.fold_in(_tk, 500 + 22), (1250, 128), jnp.float32)
        tbl_23 = 0.05 * jax.random.normal(jax.random.fold_in(_tk, 500 + 23), (1250, 128), jnp.float32)
        tbl_24 = 0.05 * jax.random.normal(jax.random.fold_in(_tk, 500 + 24), (1250, 128), jnp.float32)
        tbl_25 = 0.05 * jax.random.normal(jax.random.fold_in(_tk, 500 + 25), (1250, 128), jnp.float32)
        _rk = jax.random.fold_in(_tk, 7)
        r_dense_features = -0.000520686 + 1.00062 * jax.random.normal(jax.random.fold_in(_rk, 101), (512, 128), jnp.float32)
        W_top1 = 0.0405887 * jax.random.normal(jax.random.fold_in(_tk, 801), (607, 512), jnp.float32)
        W_top2 = 0.0441942 * jax.random.normal(jax.random.fold_in(_tk, 802), (512, 256), jnp.float32)
        W_top3 = 0.0625 * jax.random.normal(jax.random.fold_in(_tk, 803), (256, 1), jnp.float32)
        b_top1 = jnp.zeros((512,), jnp.float32)
        b_top2 = jnp.zeros((256,), jnp.float32)
        return (r_dense_features, ids, tbl_0, tbl_1, tbl_2, tbl_3, tbl_4, tbl_5, tbl_6, tbl_7, tbl_8, tbl_9, tbl_10, tbl_11, tbl_12, tbl_13, tbl_14, tbl_15, tbl_16, tbl_17, tbl_18, tbl_19, tbl_20, tbl_21, tbl_22, tbl_23, tbl_24, tbl_25, W_top1, b_top1, W_top2, b_top2, W_top3)
    r_dense_features, ids, tbl_0, tbl_1, tbl_2, tbl_3, tbl_4, tbl_5, tbl_6, tbl_7, tbl_8, tbl_9, tbl_10, tbl_11, tbl_12, tbl_13, tbl_14, tbl_15, tbl_16, tbl_17, tbl_18, tbl_19, tbl_20, tbl_21, tbl_22, tbl_23, tbl_24, tbl_25, W_top1, b_top1, W_top2, b_top2, W_top3 = _rec_inputs()

    def _L0_rec_setup():
        import jax, jax.numpy as jnp
        import numpy as np
        B, F, D = (2048, 26, 128)
        key = jax.random.key(seed)
        k1, k2 = jax.random.split(key)
        dense_features = jax.random.normal(k1, (B, D), dtype=jnp.float32)
        sparse_values = jax.random.normal(k2, (B, F, D), dtype=jnp.float32)
        return {'dense_features': dense_features, 'sparse_values': sparse_values}
    _L0_rec_all = _L0_rec_setup()
    _L0_rec_in = {k: v for k, v in _L0_rec_all.items() if k in ()}
    del _L0_rec_all
    return {'r_dense_features': r_dense_features, 'ids': ids, 'tbl_0': tbl_0, 'tbl_1': tbl_1, 'tbl_2': tbl_2, 'tbl_3': tbl_3, 'tbl_4': tbl_4, 'tbl_5': tbl_5, 'tbl_6': tbl_6, 'tbl_7': tbl_7, 'tbl_8': tbl_8, 'tbl_9': tbl_9, 'tbl_10': tbl_10, 'tbl_11': tbl_11, 'tbl_12': tbl_12, 'tbl_13': tbl_13, 'tbl_14': tbl_14, 'tbl_15': tbl_15, 'tbl_16': tbl_16, 'tbl_17': tbl_17, 'tbl_18': tbl_18, 'tbl_19': tbl_19, 'tbl_20': tbl_20, 'tbl_21': tbl_21, 'tbl_22': tbl_22, 'tbl_23': tbl_23, 'tbl_24': tbl_24, 'tbl_25': tbl_25, 'W_top1': W_top1, 'b_top1': b_top1, 'W_top2': W_top2, 'b_top2': b_top2, 'W_top3': W_top3}

def reference(r_dense_features, ids, tbl_0, tbl_1, tbl_2, tbl_3, tbl_4, tbl_5, tbl_6, tbl_7, tbl_8, tbl_9, tbl_10, tbl_11, tbl_12, tbl_13, tbl_14, tbl_15, tbl_16, tbl_17, tbl_18, tbl_19, tbl_20, tbl_21, tbl_22, tbl_23, tbl_24, tbl_25, W_top1, b_top1, W_top2, b_top2, W_top3):
    import jax
    import jax.numpy as jnp

    def _L0_rec_ref(dense_features, sparse_values):
        import jax, jax.numpy as jnp
        import numpy as np
        B, F, D = (2048, 26, 128)
        sd = jnp.einsum('bfd,bd->bf', sparse_values, dense_features)
        ss = jnp.einsum('bfd,bgd->bfg', sparse_values, sparse_values)
        iu, ju = jnp.triu_indices(F, k=1)
        pairs = ss[:, iu, ju]
        return jnp.concatenate([dense_features, sd, pairs], axis=1)
    e = jnp.stack([tbl_0[ids[:, 0]], tbl_1[ids[:, 1]], tbl_2[ids[:, 2]], tbl_3[ids[:, 3]], tbl_4[ids[:, 4]], tbl_5[ids[:, 5]], tbl_6[ids[:, 6]], tbl_7[ids[:, 7]], tbl_8[ids[:, 8]], tbl_9[ids[:, 9]], tbl_10[ids[:, 10]], tbl_11[ids[:, 11]], tbl_12[ids[:, 12]], tbl_13[ids[:, 13]], tbl_14[ids[:, 14]], tbl_15[ids[:, 15]], tbl_16[ids[:, 16]], tbl_17[ids[:, 17]], tbl_18[ids[:, 18]], tbl_19[ids[:, 19]], tbl_20[ids[:, 20]], tbl_21[ids[:, 21]], tbl_22[ids[:, 22]], tbl_23[ids[:, 23]], tbl_24[ids[:, 24]], tbl_25[ids[:, 25]]], axis=1)
    z = _L0_rec_ref(r_dense_features, e)
    z = z.reshape(z.shape[0], -1)
    h = jnp.concatenate([z, r_dense_features], axis=1)
    h = jnp.maximum(h @ W_top1 + b_top1, 0.0)
    h = jnp.maximum(h @ W_top2 + b_top2, 0.0)
    y = h @ W_top3
    return y

_drawn_inputs = setup_inputs


def setup_inputs(seed=0):
    import zlib

    import numpy as np

    out = dict(_drawn_inputs(seed))
    spreads = {'b_top1': (0.0, 0.1), 'b_top2': (0.0, 0.1)}
    factors = {}
    for name, (base, spread) in spreads.items():
        noise = np.random.default_rng([zlib.crc32(name.encode()), seed]).standard_normal(out[name].shape)
        drawn = base * np.exp(spread * noise) if base else spread * noise
        out[name] = jnp.asarray(drawn.astype(out[name].dtype))
    for name, factor in factors.items():
        out[name] = (out[name] * factor).astype(out[name].dtype)
    return out
```

```python
from contextlib import ExitStack

import concourse.bass as bass
from concourse import mybir

BATCH = 512
FEATURES = 26
DIM = 128
TILE = 128
TILES = BATCH // TILE
HIDDEN1 = 512
HIDDEN2 = 256
SLOT_PITCH = 32
ONEHOT_TABLES = [0, 3, 4, 5]
ONEHOT_ROWS = 1000
SLOTS = FEATURES + 1
GATHERED_TABLES = [f for f in range(FEATURES) if f not in ONEHOT_TABLES]
N_ONEHOT = len(ONEHOT_TABLES)
N_GATHERED = len(GATHERED_TABLES)
DENSE_SLOT = N_ONEHOT
FIRST_GATHERED_SLOT = N_ONEHOT + 1
SLOT_FEATURE = ONEHOT_TABLES + [FEATURES] + GATHERED_TABLES
COLUMNS = SLOTS - 1
PAIR_CHUNKS = -(-COLUMNS // 4)


def dlrm_tower(nc, gather_ids, onehot_ids, row_numbers, tables, dense_t, w_pairs, w_dense_a, w_dense_b,
               b1, w2, b2, w3, identity, out):
    F32, I32 = mybir.dt.float32, mybir.dt.int32
    BF16, F16 = mybir.dt.bfloat16, mybir.dt.float16
    ALU, ACT = mybir.AluOpType, mybir.ActivationFunctionType

    ROW_CHUNKS = -(-ONEHOT_ROWS // 128)
    LAST_ROWS = ONEHOT_ROWS - 128 * (ROW_CHUNKS - 1)
    PARTS = 3
    BATCH_T = 4
    BATCHES = -(-N_GATHERED // BATCH_T)
    BATCH_SIZE = [min(BATCH_T, N_GATHERED - BATCH_T * b) for b in range(BATCHES)]
    GROUP = 4
    PHASE = 8
    PHASES = TILE // GROUP // PHASE
    CHUNKS1 = HIDDEN1 // 128
    CHUNKS2 = HIDDEN2 // 128

    ctx = ExitStack()
    with ctx:
        def sb(name, shape, dt=F32):
            return ctx.enter_context(nc.sbuf_tensor(name, shape, dt))

        def pb(name, shape):
            return ctx.enter_context(nc.psum_tensor(name, shape, F32))

        def sem(name):
            return ctx.enter_context(nc.semaphore(name))

        gather_idx = sb("gather_idx", [128, TILES, N_GATHERED], I32)
        rows = sb("rows", [128, 2, N_GATHERED, DIM])
        embT = sb("embT", [128, BATCH, SLOT_PITCH])
        pairs = sb("pairs", [128, 2, PAIR_CHUNKS, TILE])
        ident = sb("ident", [128, 128])
        ids_i = sb("ids_i", [128, N_ONEHOT, BATCH], I32)
        ids_h = sb("ids_h", [128, N_ONEHOT, BATCH], F16)
        row_no = sb("row_no", [128, ROW_CHUNKS])
        table = sb("table", [128, 2, ROW_CHUNKS, DIM])
        rest = sb("rest", [128, 2, ROW_CHUNKS, DIM])
        part = sb("part", [128, 2, PARTS, ROW_CHUNKS, DIM], BF16)
        onehot = sb("onehot", [128, 2, ROW_CHUNKS, BATCH], BF16)
        denseT = sb("denseT", [128, BATCH])
        wp = sb("wp", [128, PAIR_CHUNKS, HIDDEN1])
        wda = sb("wda", [128, HIDDEN1])
        wdb = sb("wdb", [128, HIDDEN1])
        w2s = sb("w2s", [128, CHUNKS1, HIDDEN2])
        w3s = sb("w3s", [128, CHUNKS2])
        b1s = sb("b1s", [128, CHUNKS1])
        b2s = sb("b2s", [128, CHUNKS2])
        h1 = sb("h1", [128, CHUNKS1, TILE])
        h2 = sb("h2", [128, CHUNKS2, TILE])
        y = sb("y", [1, BATCH])

        turned = [pb(f"turned{i}", [128, BATCH_T, TILE]) for i in range(2)]
        dots = [pb(f"dots{i}", [128, PHASE, 128]) for i in range(2)]
        mlp = [pb(f"mlp{i}", [128, 512]) for i in range(2)]
        selected = [dots[i][:, 0:4, :].rearrange("p a b -> p (a b)") for i in range(2)]

        gather_ids_loaded = sem("gather_ids_loaded")
        ident_loaded = sem("ident_loaded")
        onehot_ids_loaded = sem("onehot_ids_loaded")
        table_loaded = [sem(f"table_loaded{i}") for i in range(2)]
        mlp_loaded = sem("mlp_loaded")
        dense_loaded = sem("dense_loaded")
        gathered = [[sem(f"gathered{i}_{b}") for b in range(BATCHES)] for i in range(2)]
        pad_zeroed = sem("pad_zeroed")
        ids_half = sem("ids_half")
        high_ready = sem("high_ready")
        rest_ready = sem("rest_ready")
        mid_ready = sem("mid_ready")
        low_ready = sem("low_ready")
        onehot_ready = sem("onehot_ready")
        table_selected = sem("table_selected")
        table_placed = [sem("table_placed_act"), sem("table_placed_dve")]
        slots_ready = sem("slots_ready")
        weights_added = sem("weights_added")
        transposed = sem("transposed")
        batch_placed = [sem("batch_placed_act"), sem("batch_placed_dve")]
        dots_done = sem("dots_done")
        dots_copied = [sem("dots_copied_act"), sem("dots_copied_dve")]
        layer1_done = sem("layer1_done")
        h1_ready = [sem("h1_ready_act"), sem("h1_ready_dve")]
        layer2_done = sem("layer2_done")
        h2_ready = [sem("h2_ready_act"), sem("h2_ready_dve")]
        layer3_done = sem("layer3_done")
        y_ready = sem("y_ready")
        stored = sem("stored")

        PROLOGUE = []
        for i in range(max(N_ONEHOT, BATCHES)):
            if i < N_ONEHOT:
                PROLOGUE.append(("table", 0, i))
            if i < BATCHES:
                PROLOGUE.append(("batch", 0, i))
        STEADY = []
        for t in range(1, TILES):
            p = t - 1
            STEADY += [("dots", p, 0), ("dots", p, 1), ("batch", t, 0), ("dots", p, 2), ("dots", p, 3),
                       ("batch", t, 1), ("layer1", p, 0), ("batch", t, 2), ("layer2", p, 0),
                       ("batch", t, 3), ("layer3", p, 0), ("batch", t, 4), ("batch", t, 5)]
        t = TILES - 1
        EPILOGUE = [("dots", t, i) for i in range(PHASES)] + [("layer1", t, 0), ("layer2", t, 0), ("layer3", t, 0)]
        STEPS = PROLOGUE + STEADY + EPILOGUE

        def batch_no(t, b):
            return t * BATCHES + b

        def placed_by(engine, n):
            return (n + 1 - engine) // 2

        block = ctx.enter_context(nc.Block())

        @block.sync
        def _(sp):
            sp.dma_start(gather_idx[:, :, :], gather_ids).then_inc(gather_ids_loaded, 16)
            sp.dma_start(ids_i[:, :, :], onehot_ids[None, :, :].broadcast_to([128, N_ONEHOT, BATCH])
                         ).then_inc(onehot_ids_loaded, 16)
            sp.dma_start(row_no[:, :], row_numbers).then_inc(onehot_ids_loaded, 16)
            full = 128 * (ROW_CHUNKS - 1)
            for i in range(N_ONEHOT):
                if i == 0:
                    sp.wait_ge(pad_zeroed, 1)
                if i >= 2:
                    sp.wait_ge(rest_ready, i - 1)
                sp.dma_start(table[:, i % 2, 0:ROW_CHUNKS - 1, :],
                             tables[ONEHOT_TABLES[i]][0:full, :].rearrange("(c p) d -> p c d", p=128)
                             ).then_inc(table_loaded[i % 2], 16)
                sp.dma_start(table[0:LAST_ROWS, i % 2, ROW_CHUNKS - 1, :],
                             tables[ONEHOT_TABLES[i]][full:ONEHOT_ROWS, :]).then_inc(table_loaded[i % 2], 16)
                if i == 0:
                    sp.dma_start(ident[:, :], identity).then_inc(ident_loaded, 16)
                if i == 1:
                    sp.dma_start(denseT[:, :], dense_t).then_inc(dense_loaded, 16)
            for dst, src in ((wp[:, :, :], w_pairs), (wda[:, :], w_dense_a), (wdb[:, :], w_dense_b),
                             (b1s[:, :], b1), (w2s[:, :, :], w2), (b2s[:, :], b2), (w3s[:, :], w3)):
                sp.dma_start(dst, src).then_inc(mlp_loaded, 16)
            sp.wait_ge(y_ready, TILES)
            sp.dma_start(out, y[0:1, :]).then_inc(stored, 16)
            sp.wait_ge(stored, 16)

        MLP_LOADED = 7 * 16

        @block.gpsimd
        def _(pool):
            pool.wait_ge(gather_ids_loaded, 16)
            for t in range(TILES):
                for n in range(N_GATHERED):
                    b = n // BATCH_T
                    if t >= 2 and n % BATCH_T == 0:
                        pool.wait_ge(transposed, batch_no(t - 2, b) + 1)
                    pool.indirect_dma_start(
                        out=rows[:, t % 2, n, :], out_offset=None, in_=tables[GATHERED_TABLES[n]][:, :],
                        in_offset=bass.IndirectOffsetOnAxis(ap=gather_idx[:, t, n:n + 1], axis=0),
                    ).then_inc(gathered[t % 2][b], 16)

        def place_table(eng, copy, engine, i):
            eng.wait_ge(table_selected, i + 1)
            copy(embT[:, :, i], selected[i % 2][:, :]).then_inc(table_placed[engine], 1)

        def place_batch(eng, copy, engine, t, b):
            eng.wait_ge(transposed, batch_no(t, b) + 1)
            n, s = BATCH_SIZE[b], FIRST_GATHERED_SLOT + BATCH_T * b
            bank = turned[batch_no(t, b) % 2]
            copy(embT[:, t * TILE:(t + 1) * TILE, s:s + n].rearrange("p b s -> p s b"),
                 bank[:, 0:n, :]).then_inc(batch_placed[engine], 1)

        def copy_dots(eng, copy, engine, t, phase):
            n = t * PHASES + phase
            eng.wait_ge(dots_done, n + 1)
            if t >= 2 and phase == 0:
                eng.wait_ge(layer1_done, t - 1)
            for j in (2 * engine, 2 * engine + 1):
                block_of_j = dots[n % 2][32 * j:32 * j + 32, :, COLUMNS * j:COLUMNS * (j + 1)]
                for r in range(4):
                    c = -(-(COLUMNS - r) // 4)
                    s0 = phase * PHASE * GROUP + j
                    last = copy(
                        pairs[32 * r:32 * r + 32, t % 2, 0:c, s0:s0 + (PHASE - 1) * GROUP + 1:GROUP]
                        .rearrange("p c g -> p g c"),
                        block_of_j[:, :, r::4])
            last.then_inc(dots_copied[engine], 1)

        @block.scalar
        def _(act):
            def copy(dst, src):
                return nc.scalar.copy(dst, src)

            def split_high(i):
                act.wait_ge(table_loaded[i % 2], 32 * (i // 2 + 1))
                if i >= 2:
                    act.wait_ge(table_selected, i - 1)
                nc.scalar.copy(part[:, i % 2, 0, :, :], table[:, i % 2, :, :]).then_inc(high_ready, 1)

            def split_mid(i):
                act.wait_ge(rest_ready, i + 1)
                nc.scalar.copy(part[:, i % 2, 1, :, :], rest[:, i % 2, :, :]).then_inc(mid_ready, 1)

            def step(kind, t, i):
                if kind == "table" and i % 2 == 0:
                    place_table(act, copy, 0, i)
                elif kind == "batch" and batch_no(t, i) % 2 == 0:
                    place_batch(act, copy, 0, t, i)
                elif kind == "dots":
                    copy_dots(act, copy, 0, t, i)
                elif kind == "layer1":
                    if t == 0:
                        act.wait_ge(mlp_loaded, MLP_LOADED)
                    act.wait_ge(layer1_done, t + 1)
                    for m in range(2):
                        last = nc.scalar.activation(h1[:, m, :], mlp[0][:, m * TILE:(m + 1) * TILE], ACT.Relu,
                                                    bias=b1s[:, m:m + 1])
                    last.then_inc(h1_ready[0], 1)
                elif kind == "layer2":
                    act.wait_ge(layer2_done, t + 1)
                    nc.scalar.activation(h2[:, 0, :], mlp[0][:, 0:TILE], ACT.Relu,
                                         bias=b2s[:, 0:1]).then_inc(h2_ready[0], 1)

            split_high(0)
            done = 0
            for i in range(N_ONEHOT):
                if i + 1 < N_ONEHOT:
                    split_high(i + 1)
                split_mid(i)
                if i:
                    step(*PROLOGUE[done])
                    step(*PROLOGUE[done + 1])
                    done += 2
            for s in STEPS[done:]:
                step(*s)

        @block.vector
        def _(dve):
            def copy(dst, src):
                return nc.vector.tensor_copy(dst, src)

            def split_and_onehot(i):
                dve.wait_ge(high_ready, i + 1)
                nc.vector.tensor_tensor(rest[:, i % 2, :, :], table[:, i % 2, :, :], part[:, i % 2, 0, :, :],
                                        ALU.subtract).then_inc(rest_ready, 1)
                if i >= 2:
                    dve.wait_ge(table_selected, i - 1)
                for c in range(ROW_CHUNKS):
                    last = nc.vector.tensor_scalar(onehot[:, i % 2, c, :], ids_h[:, i, :], row_no[:, c:c + 1],
                                                   None, ALU.is_equal)
                last.then_inc(onehot_ready, 1)
                dve.wait_ge(mid_ready, i + 1)
                nc.vector.tensor_tensor(part[:, i % 2, 2, :, :], rest[:, i % 2, :, :], part[:, i % 2, 1, :, :],
                                        ALU.subtract).then_inc(low_ready, 1)

            def step(kind, t, i):
                if kind == "table" and i % 2 == 1:
                    place_table(dve, copy, 1, i)
                elif kind == "batch" and batch_no(t, i) % 2 == 1:
                    place_batch(dve, copy, 1, t, i)
                elif kind == "dots":
                    copy_dots(dve, copy, 1, t, i)
                elif kind == "layer1":
                    dve.wait_ge(layer1_done, t + 1)
                    if t == 0:
                        dve.wait_ge(mlp_loaded, MLP_LOADED)
                    for m in range(2, 4):
                        last = nc.vector.tensor_scalar(h1[:, m, :], mlp[1][:, (m - 2) * TILE:(m - 1) * TILE],
                                                       b1s[:, m:m + 1], 0.0, ALU.add, ALU.max)
                    last.then_inc(h1_ready[1], 1)
                elif kind == "layer2":
                    dve.wait_ge(layer2_done, t + 1)
                    nc.vector.tensor_scalar(h2[:, 1, :], mlp[1][:, 0:TILE], b2s[:, 1:2], 0.0,
                                            ALU.add, ALU.max).then_inc(h2_ready[1], 1)
                elif kind == "layer3":
                    dve.wait_ge(layer3_done, t + 1)
                    nc.vector.tensor_copy(y[0:1, t * TILE:(t + 1) * TILE], mlp[0][0:1, 256:256 + TILE]
                                          ).then_inc(y_ready, 1)

            nc.vector.memset(table[:, :, ROW_CHUNKS - 1, :], 0.0).then_inc(pad_zeroed, 1)
            dve.wait_ge(onehot_ids_loaded, 32)
            nc.vector.tensor_copy(ids_h[:, :, :], ids_i[:, :, :]).then_inc(ids_half, 1)
            dve.wait_ge(ids_half, 1)
            split_and_onehot(0)
            nc.vector.memset(embT[:, :, SLOTS:SLOT_PITCH], 0.0).then_inc(slots_ready, 1)
            nc.vector.memset(pairs[64:128, :, PAIR_CHUNKS - 1, :], 0.0).then_inc(slots_ready, 1)
            dve.wait_ge(dense_loaded, 16)
            nc.vector.tensor_copy(embT[:, :, DENSE_SLOT], denseT[:, :]).then_inc(slots_ready, 1)
            done = 0
            for i in range(1, N_ONEHOT):
                split_and_onehot(i)
                step(*PROLOGUE[done])
                step(*PROLOGUE[done + 1])
                done += 2
            dve.wait_ge(mlp_loaded, MLP_LOADED)
            nc.vector.tensor_tensor(wda[:, :], wda[:, :], wdb[:, :], ALU.add).then_inc(weights_added, 1)
            for s in STEPS[done:]:
                step(*s)

        @block.tensor
        def _(pe):
            def step(kind, t, i):
                if kind == "table":
                    pe.wait_ge(onehot_ready, i + 1)
                    pe.wait_ge(mid_ready, i + 1)
                    pe.wait_ge(low_ready, i + 1)
                    if i >= 2:
                        pe.wait_ge(table_placed[i % 2], i // 2)
                    n = ROW_CHUNKS * PARTS
                    for m in range(n):
                        c, q = divmod(m, PARTS)
                        last = nc.tensor.matmul(selected[i % 2][:, :], part[:, i % 2, q, c, :],
                                                onehot[:, i % 2, c, :], start=(m == 0), stop=(m == n - 1))
                    last.then_inc(table_selected, 1)
                elif kind == "batch":
                    n = batch_no(t, i)
                    if n == 0:
                        pe.wait_ge(ident_loaded, 16)
                    pe.wait_ge(gathered[t % 2][i], 16 * BATCH_SIZE[i] * (t // 2 + 1))
                    if n >= 2:
                        pe.wait_ge(batch_placed[n % 2], n // 2)
                    for m in range(BATCH_SIZE[i]):
                        last = nc.tensor.transpose(turned[n % 2][:, m, :], rows[:, t % 2, BATCH_T * i + m, :],
                                                   ident[:, :])
                    last.then_inc(transposed, 1)
                elif kind == "dots":
                    n = t * PHASES + i
                    if i == 0:
                        for engine in range(2):
                            pe.wait_ge(batch_placed[engine], placed_by(engine, batch_no(t + 1, 0)))
                            pe.wait_ge(table_placed[engine], placed_by(engine, N_ONEHOT))
                        pe.wait_ge(slots_ready, 3)
                    if n >= 2:
                        for engine in range(2):
                            pe.wait_ge(dots_copied[engine], n - 1)
                    for g in range(PHASE):
                        s = t * TILE + (i * PHASE + g) * GROUP
                        last = nc.tensor.matmul(dots[n % 2][:, g, 0:GROUP * COLUMNS], embT[:, s:s + GROUP, :],
                                                embT[:, s:s + GROUP, 1:SLOTS], start=True, stop=True)
                    last.then_inc(dots_done, 1)
                elif kind == "layer1":
                    if t == 0:
                        pe.wait_ge(mlp_loaded, MLP_LOADED)
                        pe.wait_ge(weights_added, 1)
                    if t >= 1:
                        pe.wait_ge(y_ready, t)
                    for m in range(CHUNKS1):
                        dst = mlp[m // 2][:, (m % 2) * TILE:(m % 2 + 1) * TILE]
                        cols = slice(128 * m, 128 * (m + 1))
                        nc.tensor.matmul(dst, wda[:, cols], denseT[:, t * TILE:(t + 1) * TILE],
                                         start=True, stop=False)
                        if m == 0:
                            for engine in range(2):
                                pe.wait_ge(dots_copied[engine], (t + 1) * PHASES)
                        for c in range(PAIR_CHUNKS):
                            last = nc.tensor.matmul(dst, wp[:, c, cols], pairs[:, t % 2, c, :],
                                                    start=False, stop=(c == PAIR_CHUNKS - 1))
                    last.then_inc(layer1_done, 1)
                elif kind == "layer2":
                    for engine in range(2):
                        pe.wait_ge(h1_ready[engine], t + 1)
                    for m in range(CHUNKS2):
                        for c in range(CHUNKS1):
                            last = nc.tensor.matmul(mlp[m][:, 0:TILE], w2s[:, c, 128 * m:128 * (m + 1)],
                                                    h1[:, c, :], start=(c == 0), stop=(c == CHUNKS1 - 1))
                    last.then_inc(layer2_done, 1)
                elif kind == "layer3":
                    for engine in range(2):
                        pe.wait_ge(h2_ready[engine], t + 1)
                    for c in range(CHUNKS2):
                        last = nc.tensor.matmul(mlp[0][0:1, 256:256 + TILE], w3s[:, c:c + 1], h2[:, c, :],
                                                start=(c == 0), stop=(c == CHUNKS2 - 1))
                    last.then_inc(layer3_done, 1)

            for s in STEPS:
                step(*s)


def pair_row(a, b):
    a, b = min(a, b), max(a, b)
    if b == FEATURES:
        return DIM + a
    return DIM + FEATURES + a * (2 * FEATURES - a - 1) // 2 + b - a - 1


def kernel(**inputs):
    import numpy as np
    import concourse.bacc as bacc
    from concourse.bass_utils import run_bass_kernel_spmd

    ids = np.asarray(inputs["ids"])
    w1 = np.asarray(inputs["W_top1"])
    place = np.full((4, SLOT_PITCH, PAIR_CHUNKS), w1.shape[0])
    for k in range(COLUMNS):
        for f in range(k + 1):
            place[k % 4, f, k // 4] = pair_row(SLOT_FEATURE[f], SLOT_FEATURE[k + 1])
    padded = np.concatenate([w1, np.zeros((1, HIDDEN1), w1.dtype)])
    arrays = {
        "gather_ids": ids[:, GATHERED_TABLES].reshape(TILES, TILE, N_GATHERED).transpose(1, 0, 2),
        "onehot_ids": ids[:, ONEHOT_TABLES].T,
        "row_numbers": np.arange(128)[:, None].astype(np.float32) + 128 * np.arange(-(-ONEHOT_ROWS // 128), dtype=np.float32),
        "dense_t": np.asarray(inputs["r_dense_features"]).T,
        "w_pairs": padded[place.reshape(128, PAIR_CHUNKS)],
        "w_dense_a": w1[0:DIM],
        "w_dense_b": w1[w1.shape[0] - DIM:],
        "b1": np.asarray(inputs["b_top1"]).reshape(-1, 128).T,
        "w2": np.asarray(inputs["W_top2"]).reshape(-1, 128, HIDDEN2).transpose(1, 0, 2),
        "b2": np.asarray(inputs["b_top2"]).reshape(-1, 128).T,
        "w3": np.asarray(inputs["W_top3"]).reshape(-1, 128).T,
        "identity": np.eye(128, dtype=np.float32),
    }
    arrays |= {f"tbl_{f}": np.asarray(inputs[f"tbl_{f}"]) for f in range(FEATURES)}
    arrays = {n: np.ascontiguousarray(a) for n, a in arrays.items()}

    nc = bacc.Bacc("TRN2", target_bir_lowering=False, num_devices=1)
    aps = {n: nc.dram_tensor(n, a.shape, mybir.dt.from_np(a.dtype), kind="ExternalInput").ap()
           for n, a in arrays.items()}
    out = nc.dram_tensor("out", (1, BATCH), mybir.dt.float32, kind="ExternalOutput").ap()
    dlrm_tower(nc, aps["gather_ids"], aps["onehot_ids"], aps["row_numbers"],
               [aps[f"tbl_{f}"] for f in range(FEATURES)], aps["dense_t"], aps["w_pairs"], aps["w_dense_a"],
               aps["w_dense_b"], aps["b1"], aps["w2"], aps["b2"], aps["w3"], aps["identity"], out)
    r = run_bass_kernel_spmd(nc, [arrays], core_ids=[0])
    return r.results[0]["out"].reshape(BATCH, 1)
```

```python
from contextlib import ExitStack

import concourse.bass as bass
from concourse import mybir

BATCH = 512
FEATURES = 26
DIM = 128
TILE = 128
TILES = BATCH // TILE
HIDDEN1 = 512
HIDDEN2 = 256
SLOT_PITCH = 32
ONEHOT_TABLES = [0, 3, 4, 5, 7]
ONEHOT_ROWS = 1000
SLOTS = FEATURES + 1
GATHERED_TABLES = [f for f in range(FEATURES) if f not in ONEHOT_TABLES]
N_ONEHOT = len(ONEHOT_TABLES)
N_GATHERED = len(GATHERED_TABLES)
DENSE_SLOT = N_ONEHOT
FIRST_GATHERED_SLOT = N_ONEHOT + 1
SLOT_FEATURE = ONEHOT_TABLES + [FEATURES] + GATHERED_TABLES
COLUMNS = SLOTS - 1
PAIR_CHUNKS = -(-COLUMNS // 4)
USED_CHUNKS = [2, 4, 5, 6]


def place_of(f, k):
    if k < 8:
        return 64 + 16 * (k % 4) + 2 * f + k // 4, PAIR_CHUNKS - 1
    if k < 16:
        return 32 * (k % 4) + 2 * f + k // 4 - 2, 2
    return 32 * (k % 4) + f, k // 4


def dlrm_tower(nc, gather_ids, onehot_ids, row_numbers, tables, dense_t, w_pairs, w_dense_a, w_dense_b,
               b1, w2, b2, w3, identity, out):
    F32, I32 = mybir.dt.float32, mybir.dt.int32
    BF16, F16 = mybir.dt.bfloat16, mybir.dt.float16
    ALU, ACT = mybir.AluOpType, mybir.ActivationFunctionType

    ROW_CHUNKS = -(-ONEHOT_ROWS // 128)
    LAST_ROWS = ONEHOT_ROWS - 128 * (ROW_CHUNKS - 1)
    PARTS = 3
    BATCH_T = 4
    BATCHES = -(-N_GATHERED // BATCH_T)
    BATCH_SIZE = [min(BATCH_T, N_GATHERED - BATCH_T * b) for b in range(BATCHES)]
    GROUP = 4
    PHASE = 8
    PHASES = TILE // GROUP // PHASE
    EARLY = 20
    DOTS = [(t, i, 0, COLUMNS) for t in range(TILES - 1) for i in range(PHASES)]
    DOTS += [(TILES - 1, i, 0, EARLY) for i in range(PHASES)]
    DOTS += [(TILES - 1, i, EARLY, COLUMNS) for i in range(PHASES)]
    EARLY_BATCHES = -(-(EARLY + 1 - FIRST_GATHERED_SLOT) // BATCH_T)
    EARLY_SLOTS = min(FIRST_GATHERED_SLOT + BATCH_T * EARLY_BATCHES, SLOTS)
    CHUNKS1 = HIDDEN1 // 128
    CHUNKS2 = HIDDEN2 // 128

    ctx = ExitStack()
    with ctx:
        def sb(name, shape, dt=F32):
            return ctx.enter_context(nc.sbuf_tensor(name, shape, dt))

        def pb(name, shape):
            return ctx.enter_context(nc.psum_tensor(name, shape, F32))

        def sem(name):
            return ctx.enter_context(nc.semaphore(name))

        gather_idx = sb("gather_idx", [128, TILES, N_GATHERED], I32)
        rows = sb("rows", [128, 2, N_GATHERED, DIM])
        embT = sb("embT", [128, BATCH, SLOT_PITCH])
        pairs = sb("pairs", [128, 2, PAIR_CHUNKS, TILE])
        ident = sb("ident", [128, 128])
        ids_i = sb("ids_i", [128, N_ONEHOT, BATCH], I32)
        ids_h = sb("ids_h", [128, N_ONEHOT, BATCH], F16)
        row_no = sb("row_no", [128, ROW_CHUNKS])
        table = sb("table", [128, 2, ROW_CHUNKS, DIM])
        rest = sb("rest", [128, 2, ROW_CHUNKS, DIM])
        part = sb("part", [128, 2, PARTS, ROW_CHUNKS, DIM], BF16)
        onehot = sb("onehot", [128, 2, ROW_CHUNKS, BATCH], BF16)
        denseT = sb("denseT", [128, BATCH])
        wp = sb("wp", [128, len(USED_CHUNKS), HIDDEN1])
        wda = sb("wda", [128, HIDDEN1])
        wdb = sb("wdb", [128, HIDDEN1])
        w2s = sb("w2s", [128, CHUNKS1, HIDDEN2])
        w3s = sb("w3s", [128, CHUNKS2])
        b1s = sb("b1s", [128, CHUNKS1])
        b2s = sb("b2s", [128, CHUNKS2])
        h1 = sb("h1", [128, CHUNKS1, TILE])
        h2 = sb("h2", [128, CHUNKS2, TILE])
        y = sb("y", [1, BATCH])

        turned = [pb(f"turned{i}", [128, BATCH_T, TILE]) for i in range(2)]
        dots = [pb(f"dots{i}", [128, PHASE, 128]) for i in range(2)]
        mlp = [pb(f"mlp{i}", [128, 512]) for i in range(2)]
        selected = [dots[i][:, 0:4, :].rearrange("p a b -> p (a b)") for i in range(2)]

        spread = nc.dram_tensor("spread", (TILES, 2, 128, 2 * TILE), F32, kind="Internal").ap()

        gather_ids_loaded = sem("gather_ids_loaded")
        ident_loaded = sem("ident_loaded")
        row_no_loaded = sem("row_no_loaded")
        onehot_ids_loaded = [sem(f"onehot_ids_loaded{i}") for i in range(N_ONEHOT)]
        table_loaded = [sem(f"table_loaded{i}") for i in range(2)]
        mlp_loaded = sem("mlp_loaded")
        dense_loaded = sem("dense_loaded")
        gathered = [[sem(f"gathered{i}_{b}") for b in range(BATCHES)] for i in range(2)]
        pad_zeroed = sem("pad_zeroed")
        ids_half = sem("ids_half")
        high_ready = sem("high_ready")
        rest_ready = sem("rest_ready")
        mid_ready = sem("mid_ready")
        low_ready = sem("low_ready")
        onehot_ready = sem("onehot_ready")
        table_selected = sem("table_selected")
        table_placed = [sem("table_placed_act"), sem("table_placed_dve")]
        slots_ready = sem("slots_ready")
        weights_added = sem("weights_added")
        transposed = sem("transposed")
        batch_placed = [sem("batch_placed_act"), sem("batch_placed_dve")]
        dots_done = sem("dots_done")
        dots_copied = [sem("dots_copied_act"), sem("dots_copied_dve")]
        spread_written = sem("spread_written")
        folded = [sem(f"folded{i}") for i in range(2)]
        layer1_done = sem("layer1_done")
        h1_ready = [sem("h1_ready_act"), sem("h1_ready_dve")]
        layer2_done = sem("layer2_done")
        h2_ready = [sem("h2_ready_act"), sem("h2_ready_dve")]
        layer3_done = sem("layer3_done")
        y_ready = sem("y_ready")
        stored = sem("stored")

        PROLOGUE = []
        for i in range(max(N_ONEHOT, BATCHES)):
            if i < N_ONEHOT:
                PROLOGUE.append(("table", 0, i))
            if i < BATCHES:
                PROLOGUE.append(("batch", 0, i))

        def steps(text):
            names = {"D": "dots", "B": "batch", "P": "layer1_early", "L": "layer1", "M": "layer2", "Y": "layer3"}
            return [(names[w[0]], *map(int, w[1:].split("."))) for w in text.split()]

        STEPS = PROLOGUE + steps("""
            D0.0 D0.1 B1.0 D0.2 D0.3 B1.1 B1.2 B1.3 B1.4 B1.5
            D1.0 D1.1 B2.0 D1.2 D1.3 P0.0 L0.0 B2.1 M0.0 B2.2 Y0.0 P1.0 L1.0 B2.3 M1.0 B2.4 Y1.0 B2.5
            D2.0 D2.1 B3.0 D2.2 D2.3 B3.1 B3.2 B3.3 D3.0 D3.1 D3.2 D3.3 P2.0 L2.0 B3.4 M2.0 Y2.0 B3.5
            D3.4 D3.5 D3.6 D3.7 P3.0 L3.0 M3.0 Y3.0""")

        def dots_no(t, i):
            return [n for n, d in enumerate(DOTS) if d[0] == t][i]

        def early_after(t):
            return max(n for n, d in enumerate(DOTS) if d[0] == t and d[2] < EARLY) + 1

        def dots_after(t):
            return max(n for n, d in enumerate(DOTS) if d[0] == t) + 1

        def batch_no(t, b):
            return t * BATCHES + b

        def placed_by(engine, n):
            return (n + 1 - engine) // 2

        block = ctx.enter_context(nc.Block())

        @block.sync
        def _(sp):
            sp.dma_start(gather_idx[:, :, :], gather_ids).then_inc(gather_ids_loaded, 16)
            full = 128 * (ROW_CHUNKS - 1)
            sp.dma_start(ids_i[:, 0, :], onehot_ids[0:1, :].broadcast_to([128, BATCH])
                         ).then_inc(onehot_ids_loaded[0], 16)
            sp.dma_start(row_no[:, :], row_numbers).then_inc(row_no_loaded, 16)
            for i in range(N_ONEHOT):
                if i >= 1:
                    sp.dma_start(ids_i[:, i, :], onehot_ids[i:i + 1, :].broadcast_to([128, BATCH])
                                 ).then_inc(onehot_ids_loaded[i], 16)
                if i >= 2:
                    sp.wait_ge(rest_ready, i - 1)
                sp.dma_start(table[:, i % 2, 0:ROW_CHUNKS - 1, :],
                             tables[ONEHOT_TABLES[i]][0:full, :].rearrange("(c p) d -> p c d", p=128)
                             ).then_inc(table_loaded[i % 2], 16)
                if i == 0:
                    sp.wait_ge(pad_zeroed, 1)
                sp.dma_start(table[0:LAST_ROWS, i % 2, ROW_CHUNKS - 1, :],
                             tables[ONEHOT_TABLES[i]][full:ONEHOT_ROWS, :]).then_inc(table_loaded[i % 2], 16)
                if i == 0:
                    sp.dma_start(ident[:, :], identity).then_inc(ident_loaded, 16)
                if i == 1:
                    sp.dma_start(denseT[:, :], dense_t).then_inc(dense_loaded, 16)
            for dst, src in ((wp[:, :, :], w_pairs), (wda[:, :], w_dense_a), (wdb[:, :], w_dense_b),
                             (b1s[:, :], b1), (w2s[:, :, :], w2), (b2s[:, :], b2), (w3s[:, :], w3)):
                sp.dma_start(dst, src).then_inc(mlp_loaded, 16)
            for t in range(TILES):
                for engine in range(2):
                    sp.wait_ge(dots_copied[engine], early_after(t))
                sp.dma_start(spread[t].rearrange("h p x -> p h x"),
                             pairs[:, t % 2, 0:4, :].rearrange("p (h c) s -> p h (c s)", h=2)
                             ).then_inc(spread_written, 16)
                sp.wait_ge(spread_written, 16 * (t + 1))
                sp.dma_start(pairs[64:128, t % 2, PAIR_CHUNKS - 1, :],
                             spread[t, 0].rearrange("(r i) (c s) -> r (i c) s", r=4, c=2)[:, 0:16, :]
                             ).then_inc(folded[t % 2], 16)
                sp.dma_start(pairs[:, t % 2, 2, :],
                             spread[t, 1].rearrange("(r i) (c s) -> r (i c) s", r=4, c=2)[:, 0:32, :]
                             ).then_inc(folded[t % 2], 16)
            sp.wait_ge(y_ready, TILES)
            sp.dma_start(out, y[0:1, :]).then_inc(stored, 16)
            sp.wait_ge(stored, 16)

        FOLDS = 2
        MLP_LOADED = 7 * 16

        @block.gpsimd
        def _(pool):
            nc.gpsimd.memset(embT[:, :, SLOTS:SLOT_PITCH], 0.0).then_inc(slots_ready, 1)
            pool.wait_ge(gather_ids_loaded, 16)
            for t in range(TILES):
                for n in range(N_GATHERED):
                    b = n // BATCH_T
                    if t >= 2 and n % BATCH_T == 0:
                        pool.wait_ge(transposed, batch_no(t - 2, b) + 1)
                    pool.indirect_dma_start(
                        out=rows[:, t % 2, n, :], out_offset=None, in_=tables[GATHERED_TABLES[n]][:, :],
                        in_offset=bass.IndirectOffsetOnAxis(ap=gather_idx[:, t, n:n + 1], axis=0),
                    ).then_inc(gathered[t % 2][b], 16)

        def place_table(eng, copy, engine, i):
            eng.wait_ge(table_selected, i + 1)
            copy(embT[:, :, i], selected[i % 2][:, :]).then_inc(table_placed[engine], 1)

        def place_batch(eng, copy, engine, t, b):
            eng.wait_ge(transposed, batch_no(t, b) + 1)
            n, s = BATCH_SIZE[b], FIRST_GATHERED_SLOT + BATCH_T * b
            bank = turned[batch_no(t, b) % 2]
            copy(embT[:, t * TILE:(t + 1) * TILE, s:s + n].rearrange("p b s -> p s b"),
                 bank[:, 0:n, :]).then_inc(batch_placed[engine], 1)

        def copy_dots(eng, copy, engine, t, i):
            n = dots_no(t, i)
            _, phase, k0, k1 = DOTS[n]
            eng.wait_ge(dots_done, n + 1)
            if t >= 2 and i == 0:
                eng.wait_ge(layer1_done, t - 1)
            for j in (2 * engine, 2 * engine + 1):
                block_of_j = dots[n % 2][32 * j:32 * j + 32, :, COLUMNS * j + k0:COLUMNS * j + k1]
                for r in range(4):
                    c0, c1 = k0 // 4, -(-(k1 - r) // 4)
                    s0 = phase * PHASE * GROUP + j
                    last = copy(
                        pairs[32 * r:32 * r + 32, t % 2, c0:c1, s0:s0 + (PHASE - 1) * GROUP + 1:GROUP]
                        .rearrange("p c g -> p g c"),
                        block_of_j[:, :, r::4])
            last.then_inc(dots_copied[engine], 1)

        @block.scalar
        def _(act):
            def copy(dst, src):
                return nc.scalar.copy(dst, src)

            def halve_ids(i):
                act.wait_ge(onehot_ids_loaded[i], 16)
                nc.scalar.copy(ids_h[:, i, :], ids_i[:, i, :]).then_inc(ids_half, 1)

            def split_high(i):
                act.wait_ge(table_loaded[i % 2], 32 * (i // 2 + 1))
                if i >= 2:
                    act.wait_ge(table_selected, i - 1)
                nc.scalar.copy(part[:, i % 2, 0, :, :], table[:, i % 2, :, :]).then_inc(high_ready, 1)

            def split_mid(i):
                act.wait_ge(rest_ready, i + 1)
                nc.scalar.copy(part[:, i % 2, 1, :, :], rest[:, i % 2, :, :]).then_inc(mid_ready, 1)

            def step(kind, t, i):
                if kind == "table" and i % 2 == 0:
                    place_table(act, copy, 0, i)
                elif kind == "batch" and batch_no(t, i) % 2 == 0:
                    place_batch(act, copy, 0, t, i)
                elif kind == "dots":
                    copy_dots(act, copy, 0, t, i)
                elif kind == "layer1":
                    if t == 0:
                        act.wait_ge(mlp_loaded, MLP_LOADED)
                    act.wait_ge(layer1_done, t + 1)
                    for m in range(2):
                        last = nc.scalar.activation(h1[:, m, :], mlp[0][:, m * TILE:(m + 1) * TILE], ACT.Relu,
                                                    bias=b1s[:, m:m + 1])
                    last.then_inc(h1_ready[0], 1)
                elif kind == "layer2":
                    act.wait_ge(layer2_done, t + 1)
                    nc.scalar.activation(h2[:, 0, :], mlp[0][:, 0:TILE], ACT.Relu,
                                         bias=b2s[:, 0:1]).then_inc(h2_ready[0], 1)

            halve_ids(0)
            split_high(0)
            done = 0
            for i in range(N_ONEHOT):
                if i + 1 < N_ONEHOT:
                    halve_ids(i + 1)
                    split_high(i + 1)
                split_mid(i)
                if i:
                    step(*PROLOGUE[done])
                    step(*PROLOGUE[done + 1])
                    done += 2
            for s in STEPS[done:]:
                step(*s)

        @block.vector
        def _(dve):
            def copy(dst, src):
                return nc.vector.tensor_copy(dst, src)

            def split_and_onehot(i):
                if i >= 2:
                    dve.wait_ge(table_selected, i - 1)
                dve.wait_ge(ids_half, i + 1)
                for c in range(ROW_CHUNKS):
                    last = nc.vector.tensor_scalar(onehot[:, i % 2, c, :], ids_h[:, i, :], row_no[:, c:c + 1],
                                                   None, ALU.is_equal)
                last.then_inc(onehot_ready, 1)
                dve.wait_ge(high_ready, i + 1)
                nc.vector.tensor_tensor(rest[:, i % 2, :, :], table[:, i % 2, :, :], part[:, i % 2, 0, :, :],
                                        ALU.subtract).then_inc(rest_ready, 1)
                dve.wait_ge(mid_ready, i + 1)
                nc.vector.tensor_tensor(part[:, i % 2, 2, :, :], rest[:, i % 2, :, :], part[:, i % 2, 1, :, :],
                                        ALU.subtract).then_inc(low_ready, 1)

            def step(kind, t, i):
                if kind == "table" and i % 2 == 1:
                    place_table(dve, copy, 1, i)
                elif kind == "batch" and batch_no(t, i) % 2 == 1:
                    place_batch(dve, copy, 1, t, i)
                elif kind == "dots":
                    copy_dots(dve, copy, 1, t, i)
                elif kind == "layer1":
                    dve.wait_ge(layer1_done, t + 1)
                    if t == 0:
                        dve.wait_ge(mlp_loaded, MLP_LOADED)
                    for m in range(2, 4):
                        last = nc.vector.tensor_scalar(h1[:, m, :], mlp[1][:, (m - 2) * TILE:(m - 1) * TILE],
                                                       b1s[:, m:m + 1], 0.0, ALU.add, ALU.max)
                    last.then_inc(h1_ready[1], 1)
                elif kind == "layer2":
                    dve.wait_ge(layer2_done, t + 1)
                    nc.vector.tensor_scalar(h2[:, 1, :], mlp[1][:, 0:TILE], b2s[:, 1:2], 0.0,
                                            ALU.add, ALU.max).then_inc(h2_ready[1], 1)
                elif kind == "layer3":
                    dve.wait_ge(layer3_done, t + 1)
                    nc.vector.tensor_copy(y[0:1, t * TILE:(t + 1) * TILE], mlp[0][0:1, 256:256 + TILE]
                                          ).then_inc(y_ready, 1)

            nc.vector.memset(table[:, :, ROW_CHUNKS - 1, :], 0.0).then_inc(pad_zeroed, 1)
            dve.wait_ge(row_no_loaded, 16)
            split_and_onehot(0)
            dve.wait_ge(dense_loaded, 16)
            nc.vector.tensor_copy(embT[:, :, DENSE_SLOT], denseT[:, :]).then_inc(slots_ready, 1)
            done = 0
            for i in range(1, N_ONEHOT):
                split_and_onehot(i)
                step(*PROLOGUE[done])
                step(*PROLOGUE[done + 1])
                done += 2
            nc.vector.memset(embT[:, (TILES - 1) * TILE:, EARLY_SLOTS:SLOTS], 0.0).then_inc(slots_ready, 1)
            dve.wait_ge(mlp_loaded, MLP_LOADED)
            nc.vector.tensor_tensor(wda[:, :], wda[:, :], wdb[:, :], ALU.add).then_inc(weights_added, 1)
            for s in STEPS[done:]:
                step(*s)

        @block.tensor
        def _(pe):
            def cols(m):
                return slice(128 * m, 128 * (m + 1))

            def hidden(m):
                return mlp[m // 2][:, (m % 2) * TILE:(m % 2 + 1) * TILE]

            def step(kind, t, i):
                if kind == "table":
                    pe.wait_ge(onehot_ready, i + 1)
                    if i >= 2:
                        pe.wait_ge(table_placed[i % 2], i // 2)
                    n = ROW_CHUNKS * PARTS
                    for m in range(n):
                        q, c = divmod(m, ROW_CHUNKS)
                        if c == 0:
                            pe.wait_ge((high_ready, mid_ready, low_ready)[q], i + 1)
                        last = nc.tensor.matmul(selected[i % 2][:, :], part[:, i % 2, q, c, :],
                                                onehot[:, i % 2, c, :], start=(m == 0), stop=(m == n - 1))
                    last.then_inc(table_selected, 1)
                elif kind == "batch":
                    n = batch_no(t, i)
                    if n == 0:
                        pe.wait_ge(ident_loaded, 16)
                    pe.wait_ge(gathered[t % 2][i], 16 * BATCH_SIZE[i] * (t // 2 + 1))
                    if n >= 2:
                        pe.wait_ge(batch_placed[n % 2], n // 2)
                    for m in range(BATCH_SIZE[i]):
                        last = nc.tensor.transpose(turned[n % 2][:, m, :], rows[:, t % 2, BATCH_T * i + m, :],
                                                   ident[:, :])
                    last.then_inc(transposed, 1)
                elif kind == "dots":
                    n = dots_no(t, i)
                    _, phase, _, k1 = DOTS[n]
                    batches = EARLY_BATCHES if k1 == EARLY else BATCHES
                    for engine in range(2):
                        pe.wait_ge(batch_placed[engine], placed_by(engine, batch_no(t, batches)))
                    if n == 0:
                        for engine in range(2):
                            pe.wait_ge(table_placed[engine], placed_by(engine, N_ONEHOT))
                        pe.wait_ge(slots_ready, 3)
                    if n >= 2:
                        for engine in range(2):
                            pe.wait_ge(dots_copied[engine], n - 1)
                    for g in range(PHASE):
                        s = t * TILE + (phase * PHASE + g) * GROUP
                        last = nc.tensor.matmul(dots[n % 2][:, g, 0:GROUP * COLUMNS], embT[:, s:s + GROUP, :],
                                                embT[:, s:s + GROUP, 1:SLOTS], start=True, stop=True)
                    last.then_inc(dots_done, 1)
                elif kind == "layer1_early":
                    if t == 0:
                        pe.wait_ge(mlp_loaded, MLP_LOADED)
                        pe.wait_ge(weights_added, 1)
                    if t >= 1:
                        pe.wait_ge(y_ready, t)
                    for m in range(CHUNKS1):
                        nc.tensor.matmul(hidden(m), wda[:, cols(m)], denseT[:, t * TILE:(t + 1) * TILE],
                                         start=(m % 2 == 0), stop=False, skip_group_check=True)
                    for engine in range(2):
                        pe.wait_ge(dots_copied[engine], early_after(t))
                    pe.wait_ge(folded[t % 2], (t // 2 + 1) * FOLDS * 16)
                    for m in range(CHUNKS1):
                        for u in range(2):
                            nc.tensor.matmul(hidden(m), wp[:, u, cols(m)], pairs[:, t % 2, USED_CHUNKS[u], :],
                                             start=False, stop=False, skip_group_check=True)
                elif kind == "layer1":
                    for engine in range(2):
                        pe.wait_ge(dots_copied[engine], dots_after(t))
                    for m in range(CHUNKS1):
                        for u in range(2, len(USED_CHUNKS)):
                            last = nc.tensor.matmul(hidden(m), wp[:, u, cols(m)], pairs[:, t % 2, USED_CHUNKS[u], :],
                                                    start=False, stop=(u == len(USED_CHUNKS) - 1),
                                                    skip_group_check=True)
                    last.then_inc(layer1_done, 1)
                elif kind == "layer2":
                    for engine in range(2):
                        pe.wait_ge(h1_ready[engine], t + 1)
                    for m in range(CHUNKS2):
                        for c in range(CHUNKS1):
                            last = nc.tensor.matmul(mlp[m][:, 0:TILE], w2s[:, c, 128 * m:128 * (m + 1)],
                                                    h1[:, c, :], start=(c == 0), stop=(c == CHUNKS1 - 1))
                    last.then_inc(layer2_done, 1)
                elif kind == "layer3":
                    for engine in range(2):
                        pe.wait_ge(h2_ready[engine], t + 1)
                    for c in range(CHUNKS2):
                        last = nc.tensor.matmul(mlp[0][0:1, 256:256 + TILE], w3s[:, c:c + 1], h2[:, c, :],
                                                start=(c == 0), stop=(c == CHUNKS2 - 1))
                    last.then_inc(layer3_done, 1)

            for s in STEPS:
                step(*s)


def pair_row(a, b):
    a, b = min(a, b), max(a, b)
    if b == FEATURES:
        return DIM + a
    return DIM + FEATURES + a * (2 * FEATURES - a - 1) // 2 + b - a - 1


def kernel(**inputs):
    import numpy as np
    import concourse.bacc as bacc
    from concourse.bass_utils import run_bass_kernel_spmd

    ids = np.asarray(inputs["ids"])
    w1 = np.asarray(inputs["W_top1"])
    place = np.full((128, len(USED_CHUNKS)), w1.shape[0])
    for k in range(COLUMNS):
        for f in range(k + 1):
            partition, chunk = place_of(f, k)
            place[partition, USED_CHUNKS.index(chunk)] = pair_row(SLOT_FEATURE[f], SLOT_FEATURE[k + 1])
    padded = np.concatenate([w1, np.zeros((1, HIDDEN1), w1.dtype)])
    arrays = {
        "gather_ids": ids[:, GATHERED_TABLES].reshape(TILES, TILE, N_GATHERED).transpose(1, 0, 2),
        "onehot_ids": ids[:, ONEHOT_TABLES].T,
        "row_numbers": np.arange(128)[:, None].astype(np.float32) + 128 * np.arange(-(-ONEHOT_ROWS // 128), dtype=np.float32),
        "dense_t": np.asarray(inputs["r_dense_features"]).T,
        "w_pairs": padded[place],
        "w_dense_a": w1[0:DIM],
        "w_dense_b": w1[w1.shape[0] - DIM:],
        "b1": np.asarray(inputs["b_top1"]).reshape(-1, 128).T,
        "w2": np.asarray(inputs["W_top2"]).reshape(-1, 128, HIDDEN2).transpose(1, 0, 2),
        "b2": np.asarray(inputs["b_top2"]).reshape(-1, 128).T,
        "w3": np.asarray(inputs["W_top3"]).reshape(-1, 128).T,
        "identity": np.eye(128, dtype=np.float32),
    }
    arrays |= {f"tbl_{f}": np.asarray(inputs[f"tbl_{f}"]) for f in range(FEATURES)}
    arrays = {n: np.ascontiguousarray(a) for n, a in arrays.items()}

    nc = bacc.Bacc("TRN2", target_bir_lowering=False, num_devices=1)
    aps = {n: nc.dram_tensor(n, a.shape, mybir.dt.from_np(a.dtype), kind="ExternalInput").ap()
           for n, a in arrays.items()}
    out = nc.dram_tensor("out", (1, BATCH), mybir.dt.float32, kind="ExternalOutput").ap()
    dlrm_tower(nc, aps["gather_ids"], aps["onehot_ids"], aps["row_numbers"],
               [aps[f"tbl_{f}"] for f in range(FEATURES)], aps["dense_t"], aps["w_pairs"], aps["w_dense_a"],
               aps["w_dense_b"], aps["b1"], aps["w2"], aps["b2"], aps["w3"], aps["identity"], out)
    r = run_bass_kernel_spmd(nc, [arrays], core_ids=[0])
    return r.results[0]["out"].reshape(BATCH, 1)
```

```python
from contextlib import ExitStack

import concourse.bass as bass
from concourse import mybir

BATCH = 512
FEATURES = 26
DIM = 128
TILE = 128
TILES = BATCH // TILE
HIDDEN1 = 512
HIDDEN2 = 256
SLOT_PITCH = 32
ONEHOT_TABLES = [0, 3, 4, 5, 7, 11, 15]
ONEHOT_ROWS = 1000
ACT_CHUNKS = 1
SLOTS = FEATURES + 1
GATHERED_TABLES = [f for f in range(FEATURES) if f not in ONEHOT_TABLES]
N_ONEHOT = len(ONEHOT_TABLES)
N_GATHERED = len(GATHERED_TABLES)
DENSE_SLOT = N_ONEHOT
FIRST_GATHERED_SLOT = N_ONEHOT + 1
SLOT_FEATURE = ONEHOT_TABLES + [FEATURES] + GATHERED_TABLES
COLUMNS = SLOTS - 1
PAIR_CHUNKS = -(-COLUMNS // 4)
FOLDED_CHUNKS = [2, 4, 5, 6]
FOLDED_WEIGHTS = {2: PAIR_CHUNKS, 4: 4, 5: 5, 6: PAIR_CHUNKS + 1}
WEIGHT_CHUNKS = PAIR_CHUNKS + 2


def place_of(f, k):
    if k < 8:
        return 64 + 16 * (k % 4) + 2 * f + k // 4, PAIR_CHUNKS - 1
    if k < 16:
        return 32 * (k % 4) + 2 * f + k // 4 - 2, 2
    return 32 * (k % 4) + f, k // 4


def dlrm_tower(nc, gather_ids, onehot_ids, onehot_biases, tables, dense_t, w_pairs, w_dense_a, w_dense_b,
               b1, w2, b2, w3, identity, out):
    F32, I32 = mybir.dt.float32, mybir.dt.int32
    F16, F32R = mybir.dt.float16, mybir.dt.float32r
    ALU, ACT = mybir.AluOpType, mybir.ActivationFunctionType

    ROW_CHUNKS = -(-ONEHOT_ROWS // 128)
    DVE_CHUNKS = ROW_CHUNKS - ACT_CHUNKS
    LAST_ROWS = ONEHOT_ROWS - 128 * (ROW_CHUNKS - 1)
    UPPER_BITS = -(1 << 12)
    BATCH_T = 4
    BATCHES = -(-N_GATHERED // BATCH_T)
    BATCH_SIZE = [min(BATCH_T, N_GATHERED - BATCH_T * b) for b in range(BATCHES)]
    GROUP = 4
    DOT_ROWS = (GROUP - 1) * SLOT_PITCH + COLUMNS
    PHASE = 8
    PHASES = TILE // GROUP // PHASE
    FOLDED_TILES = TILES - 1
    WARMING = 56
    CHUNKS1 = HIDDEN1 // 128
    CHUNKS2 = HIDDEN2 // 128
    BANK_BLOCKS = CHUNKS1 - 1

    ctx = ExitStack()
    with ctx:
        def sb(name, shape, dt=F32):
            return ctx.enter_context(nc.sbuf_tensor(name, shape, dt))

        def pb(name, shape):
            return ctx.enter_context(nc.psum_tensor(name, shape, F32))

        def sem(name):
            return ctx.enter_context(nc.semaphore(name))

        gather_idx = sb("gather_idx", [128, TILES, N_GATHERED], I32)
        rows = sb("rows", [128, 2, N_GATHERED, DIM])
        embT = sb("embT", [128, BATCH, SLOT_PITCH])
        pairs = sb("pairs", [128, 2, PAIR_CHUNKS, TILE])
        ident = sb("ident", [128, 128])
        ids_i = sb("ids_i", [128, 2, BATCH], I32)
        ids_h = sb("ids_h", [128, 2, BATCH], F16)
        bias = sb("bias", [128, 2 + ACT_CHUNKS])
        distance = sb("distance", [128, BATCH], F16)
        zeros = sb("zeros", [128, 128], F16)
        table = sb("table", [128, 2, ROW_CHUNKS, DIM])
        masked = sb("masked", [128, 2, ROW_CHUNKS, DIM], I32)
        high = sb("high", [128, 2, ROW_CHUNKS, DIM], F32R)
        low = sb("low", [128, 2, ROW_CHUNKS, DIM], F32R)
        onehot = sb("onehot", [128, 2, ROW_CHUNKS, BATCH], F32R)
        denseT = sb("denseT", [128, BATCH])
        wp = sb("wp", [128, WEIGHT_CHUNKS, HIDDEN1])
        wda = sb("wda", [128, HIDDEN1])
        wdb = sb("wdb", [128, HIDDEN1])
        w2s = sb("w2s", [128, CHUNKS1, HIDDEN2])
        w3s = sb("w3s", [128, CHUNKS2])
        b1s = sb("b1s", [128, CHUNKS1])
        b2s = sb("b2s", [128, CHUNKS2])
        h1 = sb("h1", [128, CHUNKS1, TILE])
        h2 = sb("h2", [128, CHUNKS2, TILE])
        y = sb("y", [1, BATCH])

        turned = [pb(f"turned{i}", [128, BATCH_T, TILE]) for i in range(2)]
        dots = [pb(f"dots{i}", [128, PHASE, 128]) for i in range(2)]
        mlp = [pb(f"mlp{i}", [128, 512]) for i in range(2)]
        selected = [dots[i][:, 0:4, :].rearrange("p a b -> p (a b)") for i in range(2)]

        spread = nc.dram_tensor("spread", (FOLDED_TILES, 2, 128, 2 * TILE), F32, kind="Internal").ap()

        gather_ids_loaded = sem("gather_ids_loaded")
        ident_loaded = sem("ident_loaded")
        bias_loaded = sem("bias_loaded")
        onehot_ids_loaded = [sem(f"onehot_ids_loaded{i}") for i in range(2)]
        table_loaded = [sem(f"table_loaded{i}") for i in range(2)]
        mlp_loaded = sem("mlp_loaded")
        dense_loaded = sem("dense_loaded")
        gathered = [[sem(f"gathered{i}_{b}") for b in range(BATCHES)] for i in range(2)]
        zeros_ready = sem("zeros_ready")
        pad_zeroed = sem("pad_zeroed")
        ids_relative = sem("ids_relative")
        high_ready = sem("high_ready")
        masked_ready = sem("masked_ready")
        low_ready = sem("low_ready")
        onehot_ready = [sem("onehot_ready_act"), sem("onehot_ready_dve")]
        distance_ready = sem("distance_ready")
        table_selected = sem("table_selected")
        table_placed = sem("table_placed")
        slots_ready = sem("slots_ready")
        weights_added = sem("weights_added")
        transposed = sem("transposed")
        batch_placed = [sem("batch_placed_act"), sem("batch_placed_dve")]
        pairs_zeroed = sem("pairs_zeroed")
        dots_done = sem("dots_done")
        dots_copied = [sem("dots_copied_act"), sem("dots_copied_dve")]
        spread_written = sem("spread_written")
        folded = [sem(f"folded{i}") for i in range(2)]
        layer1_done = sem("layer1_done")
        h1_ready = [sem("h1_ready_act"), sem("h1_ready_dve")]
        layer2_done = sem("layer2_done")
        h2_ready = [sem("h2_ready_act"), sem("h2_ready_dve")]
        layer3_done = sem("layer3_done")
        y_ready = sem("y_ready")
        stored = sem("stored")

        PROLOGUE = []
        for i in range(max(N_ONEHOT, BATCHES)):
            if i < N_ONEHOT:
                PROLOGUE.append(("table", 0, i))
            if i < BATCHES:
                PROLOGUE.append(("batch", 0, i))

        def steps(text):
            names = {"D": "dots", "B": "batch", "P": "layer1_dense", "L": "layer1", "M": "layer2", "Y": "layer3"}
            return [(names[w[0]], *map(int, w[1:].split("."))) for w in text.split()]

        STEPS = PROLOGUE + steps("""
            B1.0 B1.1 D0.0 D0.1 D0.2 D0.3 B1.2 B1.3 P0.0 B1.4
            D1.0 D1.1 B2.0 D1.2 D1.3 B2.1 L0.0 L0.1 M0.0 B2.2 Y0.0 B2.3 P1.0 L1.0 B2.4
            D2.0 D2.1 B3.0 D2.2 D2.3 L1.1 M1.0 B3.1 Y1.0 B3.2 P2.0 L2.0 L2.1 B3.3 M2.0 B3.4 Y2.0
            D3.0 D3.1 D3.2 D3.3 P3.0 L3.0 L3.1 M3.0 Y3.0""")

        def dots_no(t, i):
            return t * PHASES + i

        def batch_no(t, b):
            return t * BATCHES + b

        def batch_placer(n):
            return 0 if n < BATCHES else n % 2

        def placed_by(engine, n):
            return sum(batch_placer(b) == engine for b in range(n))

        MLP_LOADS = [(wda[:, :], w_dense_a), (wdb[:, :], w_dense_b), (b1s[:, :], b1), (b2s[:, :], b2),
                     (w3s[:, :], w3), (w2s[:, :, :], w2)]
        MLP_LOADS += [(wp[:, c, :], w_pairs[:, c, :]) for c in range(WEIGHT_CHUNKS)]
        MLP_LOADED = 16 * len(MLP_LOADS)
        FOLDS = 2

        block = ctx.enter_context(nc.Block())

        @block.sync
        def _(sp):
            def load_ids(i):
                sp.dma_start(ids_i[:, i % 2, :], onehot_ids[i:i + 1, :].broadcast_to([128, BATCH])
                             ).then_inc(onehot_ids_loaded[i % 2], 16)

            sp.dma_start(gather_idx[:, :, :], gather_ids).then_inc(gather_ids_loaded, 16)
            full = 128 * (ROW_CHUNKS - 1)
            for i in range(N_ONEHOT):
                if i >= 2:
                    sp.wait_ge(ids_relative, i - 1)
                if i >= 1:
                    load_ids(i)
                if i >= 2:
                    sp.wait_ge(low_ready, i - 1)
                sp.dma_start(table[:, i % 2, 0:ROW_CHUNKS - 1, :],
                             tables[ONEHOT_TABLES[i]][0:full, :].rearrange("(c p) d -> p c d", p=128)
                             ).then_inc(table_loaded[i % 2], 16)
                if i == 0:
                    sp.wait_ge(pad_zeroed, 1)
                sp.dma_start(table[0:LAST_ROWS, i % 2, ROW_CHUNKS - 1, :],
                             tables[ONEHOT_TABLES[i]][full:ONEHOT_ROWS, :]).then_inc(table_loaded[i % 2], 16)
                if i == 0:
                    load_ids(0)
                    sp.dma_start(bias[:, :], onehot_biases).then_inc(bias_loaded, 16)
                    sp.dma_start(ident[:, :], identity).then_inc(ident_loaded, 16)
                if i == 1:
                    sp.dma_start(denseT[:, :], dense_t).then_inc(dense_loaded, 16)
            for dst, src in MLP_LOADS:
                sp.dma_start(dst, src).then_inc(mlp_loaded, 16)
            for t in range(FOLDED_TILES):
                for engine in range(2):
                    sp.wait_ge(dots_copied[engine], dots_no(t + 1, 0))
                sp.dma_start(spread[t].rearrange("h p x -> p h x"),
                             pairs[:, t % 2, 0:4, :].rearrange("p (h c) s -> p h (c s)", h=2)
                             ).then_inc(spread_written, 16)
                sp.wait_ge(spread_written, 16 * (t + 1))
                sp.dma_start(pairs[64:128, t % 2, PAIR_CHUNKS - 1, :],
                             spread[t, 0].rearrange("(r i) (c s) -> r (i c) s", r=4, c=2)[:, 0:16, :]
                             ).then_inc(folded[t % 2], 16)
                sp.dma_start(pairs[:, t % 2, 2, :],
                             spread[t, 1].rearrange("(r i) (c s) -> r (i c) s", r=4, c=2)[:, 0:32, :]
                             ).then_inc(folded[t % 2], 16)
            sp.wait_ge(y_ready, TILES)
            sp.dma_start(out, y[0:1, :]).then_inc(stored, 16)
            sp.wait_ge(stored, 16)

        @block.gpsimd
        def _(pool):
            nc.gpsimd.memset(embT[:, :, SLOTS:SLOT_PITCH], 0.0).then_inc(slots_ready, 1)
            pool.wait_ge(gather_ids_loaded, 16)
            for t in range(TILES):
                for n in range(N_GATHERED):
                    b = n // BATCH_T
                    if t >= 2 and n % BATCH_T == 0:
                        pool.wait_ge(transposed, batch_no(t - 2, b) + 1)
                    pool.indirect_dma_start(
                        out=rows[:, t % 2, n, :], out_offset=None, in_=tables[GATHERED_TABLES[n]][:, :],
                        in_offset=bass.IndirectOffsetOnAxis(ap=gather_idx[:, t, n:n + 1], axis=0),
                    ).then_inc(gathered[t % 2][b], 16)

        def hidden(m):
            return mlp[m // BANK_BLOCKS][:, (m % BANK_BLOCKS) * TILE:(m % BANK_BLOCKS + 1) * TILE]

        def place_batch(eng, copy, engine, t, b):
            eng.wait_ge(transposed, batch_no(t, b) + 1)
            n, s = BATCH_SIZE[b], FIRST_GATHERED_SLOT + BATCH_T * b
            bank = turned[batch_no(t, b) % 2]
            copy(embT[:, t * TILE:(t + 1) * TILE, s:s + n].rearrange("p b s -> p s b"),
                 bank[:, 0:n, :]).then_inc(batch_placed[engine], 1)

        def copy_dots(eng, copy, engine, t, i):
            n = dots_no(t, i)
            eng.wait_ge(dots_done, n + 1)
            if n == 0:
                eng.wait_ge(pairs_zeroed, 1)
            if t >= 2 and i == 0:
                eng.wait_ge(layer1_done, 2 * (t - 1))
            for j in (2 * engine, 2 * engine + 1):
                height = 32 if j < GROUP - 1 else COLUMNS
                block_of_j = dots[n % 2][32 * j:32 * j + height, :, COLUMNS * j:COLUMNS * (j + 1)]
                for r in range(4):
                    chunks = -(-(COLUMNS - r) // 4)
                    s0 = i * PHASE * GROUP + j
                    last = copy(
                        pairs[32 * r:32 * r + height, t % 2, 0:chunks, s0:s0 + (PHASE - 1) * GROUP + 1:GROUP]
                        .rearrange("p c g -> p g c"),
                        block_of_j[:, :, r::4])
            last.then_inc(dots_copied[engine], 1)

        @block.scalar
        def _(act):
            def copy(dst, src):
                return nc.scalar.copy(dst, src)

            def relate_ids(i):
                act.wait_ge(onehot_ids_loaded[i % 2], 16 * (i // 2 + 1))
                if i >= 2:
                    act.wait_ge(onehot_ready[1], DVE_CHUNKS * (i - 1))
                nc.scalar.activation(ids_h[:, i % 2, :], ids_i[:, i % 2, :], ACT.Identity,
                                     bias=bias[:, 0:1]).then_inc(ids_relative, 1)

            def make_onehot(i):
                act.wait_ge(ids_relative, i + 1)
                if i >= 2:
                    act.wait_ge(table_selected, i - 1)
                for n in range(ACT_CHUNKS):
                    m = i * ACT_CHUNKS + n
                    if m >= 1:
                        act.wait_ge(onehot_ready[0], m)
                    nc.scalar.activation(distance[:, :], ids_h[:, i % 2, :], ACT.Abs,
                                         bias=bias[:, 2 + n:3 + n]).then_inc(distance_ready, 1)
                    act.wait_ge(distance_ready, m + 1)
                    nc.scalar.activation(onehot[:, i % 2, DVE_CHUNKS + n, :], distance[:, :], ACT.Relu,
                                         bias=bias[:, 1:2], scale=-1.0).then_inc(onehot_ready[0], 1)

            def split_high(i):
                act.wait_ge(masked_ready, i + 1)
                if i >= 2:
                    act.wait_ge(table_selected, i - 1)
                nc.scalar.copy(high[:, i % 2, :, :], masked[:, i % 2, :, :].bitcast(F32)).then_inc(high_ready, 1)

            def step(kind, t, i):
                if kind == "table":
                    act.wait_ge(table_selected, i + 1)
                    nc.scalar.copy(embT[:, :, i], selected[i % 2][:, :]).then_inc(table_placed, 1)
                elif kind == "batch" and batch_placer(batch_no(t, i)) == 0:
                    place_batch(act, copy, 0, t, i)
                elif kind == "dots":
                    copy_dots(act, copy, 0, t, i)
                elif kind == "layer1" and i == 1:
                    if t == 0:
                        act.wait_ge(mlp_loaded, MLP_LOADED)
                    act.wait_ge(layer1_done, 2 * t + 1)
                    for m in range(BANK_BLOCKS):
                        last = nc.scalar.activation(h1[:, m, :], hidden(m), ACT.Relu, bias=b1s[:, m:m + 1])
                    last.then_inc(h1_ready[0], 1)
                elif kind == "layer2":
                    act.wait_ge(layer2_done, CHUNKS2 * t + 1)
                    nc.scalar.activation(h2[:, 0, :], mlp[0][:, 0:TILE], ACT.Relu,
                                         bias=b2s[:, 0:1]).then_inc(h2_ready[0], 1)

            act.wait_ge(zeros_ready, 1)
            nc.scalar.activation(distance[:, 0:128], zeros[:, :], ACT.Identity)
            act.wait_ge(bias_loaded, 16)
            relate_ids(0)
            done = 0
            for i in range(N_ONEHOT):
                split_high(i)
                make_onehot(i)
                if i + 1 < N_ONEHOT:
                    relate_ids(i + 1)
                if i:
                    step(*PROLOGUE[done])
                    step(*PROLOGUE[done + 1])
                    done += 2
            for s in STEPS[done:]:
                step(*s)

        @block.vector
        def _(dve):
            def copy(dst, src):
                return nc.vector.tensor_copy(dst, src)

            def make_onehot(i):
                if i >= 2:
                    dve.wait_ge(table_selected, i - 1)
                dve.wait_ge(ids_relative, i + 1)
                for c in range(DVE_CHUNKS):
                    nc.vector.tensor_scalar(onehot[:, i % 2, c, :], ids_h[:, i % 2, :], float(128 * c),
                                            None, ALU.is_equal).then_inc(onehot_ready[1], 1)

            def mask_table(i):
                dve.wait_ge(table_loaded[i % 2], 32 * (i // 2 + 1))
                if i >= 2:
                    dve.wait_ge(high_ready, i - 1)
                nc.vector.tensor_scalar(masked[:, i % 2, :, :], table[:, i % 2, :, :].bitcast(I32), UPPER_BITS,
                                        None, ALU.bitwise_and).then_inc(masked_ready, 1)

            def split_low(i):
                dve.wait_ge(masked_ready, i + 1)
                if i >= 2:
                    dve.wait_ge(table_selected, i - 1)
                nc.vector.tensor_tensor(low[:, i % 2, :, :], table[:, i % 2, :, :],
                                        masked[:, i % 2, :, :].bitcast(F32), ALU.subtract).then_inc(low_ready, 1)

            def step(kind, t, i):
                if kind == "batch" and batch_placer(batch_no(t, i)) == 1:
                    place_batch(dve, copy, 1, t, i)
                elif kind == "dots":
                    copy_dots(dve, copy, 1, t, i)
                elif kind == "layer1" and i == 1:
                    if t == 0:
                        dve.wait_ge(mlp_loaded, MLP_LOADED)
                    dve.wait_ge(layer1_done, 2 * (t + 1))
                    for m in range(BANK_BLOCKS, CHUNKS1):
                        last = nc.vector.tensor_scalar(h1[:, m, :], hidden(m), b1s[:, m:m + 1], 0.0,
                                                       ALU.add, ALU.max)
                    last.then_inc(h1_ready[1], 1)
                elif kind == "layer2":
                    dve.wait_ge(layer2_done, CHUNKS2 * (t + 1))
                    nc.vector.tensor_scalar(h2[:, 1, :], mlp[1][:, 0:TILE], b2s[:, 1:2], 0.0,
                                            ALU.add, ALU.max).then_inc(h2_ready[1], 1)
                elif kind == "layer3":
                    dve.wait_ge(layer3_done, t + 1)
                    nc.vector.tensor_copy(y[0:1, t * TILE:(t + 1) * TILE], mlp[0][0:1, 3 * TILE:4 * TILE]
                                          ).then_inc(y_ready, 1)

            nc.vector.memset(zeros[:, :], 0.0).then_inc(zeros_ready, 1)
            nc.vector.memset(table[:, :, ROW_CHUNKS - 1, :], 0.0).then_inc(pad_zeroed, 1)
            nc.vector.memset(pairs[:, :, :, :], 0.0).then_inc(pairs_zeroed, 1)
            for i in range(N_ONEHOT):
                mask_table(i)
                split_low(i)
                make_onehot(i)
            dve.wait_ge(dense_loaded, 16)
            nc.vector.tensor_copy(embT[:, :, DENSE_SLOT], denseT[:, :]).then_inc(slots_ready, 1)
            dve.wait_ge(mlp_loaded, MLP_LOADED)
            nc.vector.tensor_tensor(wda[:, :], wda[:, :], wdb[:, :], ALU.add).then_inc(weights_added, 1)
            for s in STEPS:
                step(*s)

        @block.tensor
        def _(pe):
            def cols(m):
                return slice(128 * m, 128 * (m + 1))

            def step(kind, t, i):
                if kind == "table":
                    if i >= 2:
                        pe.wait_ge(table_placed, i - 1)
                    for c in range(ROW_CHUNKS):
                        if c < DVE_CHUNKS:
                            pe.wait_ge(onehot_ready[1], i * DVE_CHUNKS + c + 1)
                        else:
                            pe.wait_ge(onehot_ready[0], i * ACT_CHUNKS + c - DVE_CHUNKS + 1)
                        for part, ready in ((high, high_ready), (low, low_ready)):
                            if c == 0:
                                pe.wait_ge(ready, i + 1)
                            last = nc.tensor.matmul(selected[i % 2][:, :], part[:, i % 2, c, :], onehot[:, i % 2, c, :],
                                                    start=(part is high and c == 0),
                                                    stop=(part is low and c == ROW_CHUNKS - 1))
                    last.then_inc(table_selected, 1)
                elif kind == "batch":
                    n = batch_no(t, i)
                    if n == 0:
                        pe.wait_ge(ident_loaded, 16)
                    pe.wait_ge(gathered[t % 2][i], 16 * BATCH_SIZE[i] * (t // 2 + 1))
                    if n >= 2:
                        placer = batch_placer(n - 2)
                        pe.wait_ge(batch_placed[placer], placed_by(placer, n - 1))
                    for m in range(BATCH_SIZE[i]):
                        last = nc.tensor.transpose(turned[n % 2][:, m, :], rows[:, t % 2, BATCH_T * i + m, :],
                                                   ident[:, :])
                    last.then_inc(transposed, 1)
                elif kind == "dots":
                    n = dots_no(t, i)
                    if i == 0:
                        for engine in range(2):
                            pe.wait_ge(batch_placed[engine], placed_by(engine, batch_no(t + 1, 0)))
                    if n == 0:
                        pe.wait_ge(table_placed, N_ONEHOT)
                        pe.wait_ge(slots_ready, 2)
                    if n >= 2:
                        for engine in range(2):
                            pe.wait_ge(dots_copied[engine], n - 1)
                    for g in range(PHASE):
                        s = t * TILE + (i * PHASE + g) * GROUP
                        last = nc.tensor.matmul(dots[n % 2][0:DOT_ROWS, g, 0:GROUP * COLUMNS],
                                                embT[:, s:s + GROUP, :].rearrange("p s k -> p (s k)")[:, 0:DOT_ROWS],
                                                embT[:, s:s + GROUP, 1:SLOTS], start=True, stop=True)
                    last.then_inc(dots_done, 1)
                elif kind == "layer1_dense":
                    if t == 0:
                        pe.wait_ge(mlp_loaded, MLP_LOADED)
                        pe.wait_ge(weights_added, 1)
                    if t >= 1:
                        pe.wait_ge(y_ready, t)
                    for m in range(CHUNKS1):
                        nc.tensor.matmul(hidden(m), wda[:, cols(m)], denseT[:, t * TILE:(t + 1) * TILE],
                                         start=(m % BANK_BLOCKS == 0), stop=False, skip_group_check=True)
                elif kind == "layer1":
                    if i == 0:
                        for engine in range(2):
                            pe.wait_ge(dots_copied[engine], dots_no(t + 1, 0))
                        if t < FOLDED_TILES:
                            pe.wait_ge(folded[t % 2], (t // 2 + 1) * FOLDS * 16)
                    if t < FOLDED_TILES:
                        chunks = [(FOLDED_WEIGHTS[c], c) for c in FOLDED_CHUNKS]
                    else:
                        chunks = [(c, c) for c in range(PAIR_CHUNKS)]
                    for m in range(i * CHUNKS1 // 2, (i + 1) * CHUNKS1 // 2):
                        for w, c in chunks:
                            last = nc.tensor.matmul(hidden(m), wp[:, w, cols(m)], pairs[:, t % 2, c, :],
                                                    start=False, stop=(c == PAIR_CHUNKS - 1), skip_group_check=True)
                        if m >= BANK_BLOCKS - 1:
                            last.then_inc(layer1_done, 1)
                elif kind == "layer2":
                    pe.wait_ge(h1_ready[0], t + 1)
                    for m in range(CHUNKS2):
                        for c in range(CHUNKS1):
                            if m == 0 and c == BANK_BLOCKS:
                                pe.wait_ge(h1_ready[1], t + 1)
                            last = nc.tensor.matmul(mlp[m][:, 0:TILE], w2s[:, c, 128 * m:128 * (m + 1)],
                                                    h1[:, c, :], start=(c == 0), stop=(c == CHUNKS1 - 1))
                        last.then_inc(layer2_done, 1)
                elif kind == "layer3":
                    for c in range(CHUNKS2):
                        pe.wait_ge(h2_ready[c], t + 1)
                        last = nc.tensor.matmul(mlp[0][0:1, 3 * TILE:4 * TILE], w3s[:, c:c + 1], h2[:, c, :],
                                                start=(c == 0), stop=(c == CHUNKS2 - 1))
                    last.then_inc(layer3_done, 1)

            pe.wait_ge(zeros_ready, 1)
            for _ in range(WARMING):
                nc.tensor.matmul(mlp[0][:, 0:128], zeros[:, :], zeros[:, :], start=True, stop=True)
            for s in STEPS:
                step(*s)


def pair_row(a, b):
    a, b = min(a, b), max(a, b)
    if b == FEATURES:
        return DIM + a
    return DIM + FEATURES + a * (2 * FEATURES - a - 1) // 2 + b - a - 1


def kernel(**inputs):
    import numpy as np
    import concourse.bacc as bacc
    from concourse.bass_utils import run_bass_kernel_spmd

    ids = np.asarray(inputs["ids"])
    w1 = np.asarray(inputs["W_top1"])
    place = np.full((128, WEIGHT_CHUNKS), w1.shape[0])
    for k in range(COLUMNS):
        for f in range(k + 1):
            row = pair_row(SLOT_FEATURE[f], SLOT_FEATURE[k + 1])
            place[32 * (k % 4) + f, k // 4] = row
            partition, chunk = place_of(f, k)
            place[partition, FOLDED_WEIGHTS[chunk]] = row
    padded = np.concatenate([w1, np.zeros((1, HIDDEN1), w1.dtype)])
    arrays = {
        "gather_ids": ids[:, GATHERED_TABLES].reshape(TILES, TILE, N_GATHERED).transpose(1, 0, 2),
        "onehot_ids": ids[:, ONEHOT_TABLES].T,
        "onehot_biases": np.stack([-np.arange(128), np.ones(128)] + [
            np.full(128, -128 * (-(-ONEHOT_ROWS // 128) - ACT_CHUNKS + n)) for n in range(ACT_CHUNKS)
        ], axis=1).astype(np.float32),
        "dense_t": np.asarray(inputs["r_dense_features"]).T,
        "w_pairs": padded[place],
        "w_dense_a": w1[0:DIM],
        "w_dense_b": w1[w1.shape[0] - DIM:],
        "b1": np.asarray(inputs["b_top1"]).reshape(-1, 128).T,
        "w2": np.asarray(inputs["W_top2"]).reshape(-1, 128, HIDDEN2).transpose(1, 0, 2),
        "b2": np.asarray(inputs["b_top2"]).reshape(-1, 128).T,
        "w3": np.asarray(inputs["W_top3"]).reshape(-1, 128).T,
        "identity": np.eye(128, dtype=np.float32),
    }
    arrays |= {f"tbl_{f}": np.asarray(inputs[f"tbl_{f}"]) for f in range(FEATURES)}
    arrays = {n: np.ascontiguousarray(a) for n, a in arrays.items()}

    nc = bacc.Bacc("TRN2", target_bir_lowering=False, num_devices=1)
    aps = {n: nc.dram_tensor(n, a.shape, mybir.dt.from_np(a.dtype), kind="ExternalInput").ap()
           for n, a in arrays.items()}
    out = nc.dram_tensor("out", (1, BATCH), mybir.dt.float32, kind="ExternalOutput").ap()
    dlrm_tower(nc, aps["gather_ids"], aps["onehot_ids"], aps["onehot_biases"],
               [aps[f"tbl_{f}"] for f in range(FEATURES)], aps["dense_t"], aps["w_pairs"], aps["w_dense_a"],
               aps["w_dense_b"], aps["b1"], aps["w2"], aps["b2"], aps["w3"], aps["identity"], out)
    r = run_bass_kernel_spmd(nc, [arrays], core_ids=[0])
    return r.results[0]["out"].reshape(BATCH, 1)
```
